# Optimizing a Trainium2 kernel written in Bass

```python
import numpy as np
import jax
import jax.numpy as jnp

def _softmax(x, axis=-1):
    return jax.nn.softmax(x, axis=axis)

def _gelu(x):
    return jax.nn.gelu(x, approximate=True)

def _silu(x):
    return jax.nn.silu(x)

def _sigmoid(x):
    return jax.nn.sigmoid(x)

def _layernorm(x, axis=-1, eps=1e-05):
    m = jnp.mean(x, axis=axis, keepdims=True)
    v = jnp.var(x, axis=axis, keepdims=True)
    return (x - m) / jnp.sqrt(v + eps)

def _scatter_add(tgt, idx, src, axis=0):
    return tgt.at[idx].add(src)

def _segment_sum(src, seg, n):
    return jax.ops.segment_sum(src, seg, n)
kernel_name = 'mk_gnn_resnorm_d2_gnn_r8_207269'

def setup_inputs(seed: int=0):
    np.random.seed(seed)
    _w = jnp.asarray

    def _rec_inputs():
        import jax
        import jax.numpy as jnp
        _gk = jax.random.key(seed)
        x = -0.000202 + 1 * jax.random.normal(jax.random.fold_in(_gk, 1), (12500, 128), jnp.float32)
        src = jax.random.randint(jax.random.fold_in(_gk, 2), (200000,), 0, 12500, jnp.int32)
        dst = jax.random.randint(jax.random.fold_in(_gk, 3), (200000,), 0, 12500, jnp.int32)
        _o = jnp.argsort(dst, stable=True)
        src = src[_o]
        dst = dst[_o]
        edge_attr_4 = 0.00109026 + 0.999989 * jax.random.normal(jax.random.fold_in(_gk, 12), (200000, 4), jnp.float32)
        edge_attr_64 = 0.000103221 + 1.00003 * jax.random.normal(jax.random.fold_in(_gk, 13), (200000, 64), jnp.float32)
        edge_weight = jax.random.uniform(jax.random.fold_in(_gk, 14), (200000,), jnp.float32, 0.0, 0.799017)
        node_vec1 = jax.random.uniform(jax.random.fold_in(_gk, 15), (12500, 1), jnp.float32, 0.0, 1)
        return (x, src, dst, edge_attr_4, edge_attr_64, edge_weight, node_vec1)
    x, src, dst, edge_attr_4, edge_attr_64, edge_weight, node_vec1 = _rec_inputs()

    def _L0_gnn_setup():
        import jax, jax.numpy as jnp
        import numpy as np
        N_NODES = 6250
        N_EDGES = 100000
        DIM_IN = 128
        DIM_OUT = 128
        EPS = 1e-09

        def _branch(x, W, b, scale, offset, idx):
            h = jax.nn.relu(x @ W.T + b)
            mean = jnp.mean(h, axis=1, keepdims=True)
            var = jnp.var(h, axis=1, keepdims=True) + EPS
            d = h.shape[1]
            s = scale[idx * d:(idx + 1) * d]
            o = offset[idx * d:(idx + 1) * d]
            return (h - mean) * s * jax.lax.rsqrt(var) + o
        key = jax.random.key(seed)
        ks = jax.random.split(key, 8)
        feat_in = jax.random.normal(ks[0], (N_NODES, DIM_IN), dtype=jnp.float32)
        edge_row = jax.random.randint(ks[1], (N_EDGES,), 0, N_NODES, dtype=jnp.int32)
        edge_col = jax.random.randint(ks[2], (N_EDGES,), 0, N_NODES, dtype=jnp.int32)
        raw = jax.random.uniform(ks[3], (N_EDGES,), dtype=jnp.float32) + 0.1
        row_sum = jax.ops.segment_sum(raw, edge_row, num_segments=N_NODES)
        edge_val = raw / jnp.maximum(row_sum, EPS)[edge_row]
        W_self = jax.random.normal(ks[4], (DIM_OUT, DIM_IN), dtype=jnp.float32) * (1.0 / np.sqrt(DIM_IN))
        b_self = jax.random.normal(ks[5], (DIM_OUT,), dtype=jnp.float32) * 0.01
        W_neigh = jax.random.normal(ks[6], (DIM_OUT, DIM_IN), dtype=jnp.float32) * (1.0 / np.sqrt(DIM_IN))
        b_neigh = jax.random.normal(ks[7], (DIM_OUT,), dtype=jnp.float32) * 0.01
        scale = jnp.ones((2 * DIM_OUT,), dtype=jnp.float32)
        offset = jnp.zeros((2 * DIM_OUT,), dtype=jnp.float32)
        return {'feat_in': feat_in, 'edge_row': edge_row, 'edge_col': edge_col, 'edge_val': edge_val, 'W_self': W_self, 'b_self': b_self, 'W_neigh': W_neigh, 'b_neigh': b_neigh, 'scale': scale, 'offset': offset}
    _L0_gnn_all = _L0_gnn_setup()
    _L0_gnn_in = {k: v for k, v in _L0_gnn_all.items() if k in ('W_self', 'b_self', 'W_neigh', 'b_neigh', 'scale', 'offset')}
    del _L0_gnn_all

    def _L1_gnn_setup():
        import jax, jax.numpy as jnp
        import numpy as np
        MUL = 32
        N_NODES = 6250
        N_EDGES = 100000
        NUM_NEIGHBORS = 16.0
        SQRT3 = 3.0 ** 0.5
        SILU_NORM = 1.679

        def split_irreps(x):
            x0 = x[..., :MUL]
            x1 = x[..., MUL:].reshape(x.shape[:-1] + (MUL, 3))
            return (x0, x1)

        def merge_irreps(x0, x1):
            return jnp.concatenate([x0, x1.reshape(x1.shape[:-2] + (MUL * 3,))], axis=-1)

        def fctp_scalar(x0, x1, a, W0, W1, fan_in):
            s = a / jnp.sqrt(jnp.asarray(fan_in, x0.dtype))
            o0 = x0 @ W0 * s
            o1 = jnp.einsum('nud,uw->nwd', x1, W1) * s[..., None]
            return (o0, o1)
        key = jax.random.key(seed)
        ks = jax.random.split(key, 17)
        inp = dict(node_input=jax.random.normal(ks[0], (N_NODES, 4 * MUL), jnp.float32), node_attr=jnp.ones((N_NODES, 1), jnp.float32), edge_src=jax.random.randint(ks[1], (N_EDGES,), 0, N_NODES), edge_dst=jax.random.randint(ks[2], (N_EDGES,), 0, N_NODES), edge_attr=jax.random.normal(ks[3], (N_EDGES, 4), jnp.float32), edge_scalars=jax.random.normal(ks[4], (N_EDGES, 64), jnp.float32))
        p = lambda k, sh: jax.random.normal(k, sh, jnp.float32)
        inp.update(W_sc0=p(ks[5], (MUL, MUL)), W_sc1=p(ks[6], (MUL, MUL)), W_l1_0=p(ks[7], (MUL, MUL)), W_l1_1=p(ks[8], (MUL, MUL)), W_fc1=p(ks[9], (64, 64)), W_fc2=p(ks[10], (64, 4 * MUL)), W_l2_A0=p(ks[11], (MUL, MUL)), W_l2_B0=p(ks[12], (MUL, MUL)), W_l2_C1=p(ks[13], (MUL, MUL)), W_l2_D1=p(ks[14], (MUL, MUL)), W_l3_A=p(ks[15], (MUL, 1)), W_l3_B=p(ks[16], (MUL, 1)))
        return inp
    _L1_gnn_all = _L1_gnn_setup()
    _L1_gnn_in = {k: v for k, v in _L1_gnn_all.items() if k in ('W_sc0', 'W_sc1', 'W_l1_0', 'W_l1_1', 'W_fc1', 'W_fc2', 'W_l2_A0', 'W_l2_B0', 'W_l2_C1', 'W_l2_D1', 'W_l3_A', 'W_l3_B')}
    del _L1_gnn_all
    return {'x': x, 'src': src, 'dst': dst, 'edge_attr_4': edge_attr_4, 'edge_attr_64': edge_attr_64, 'edge_weight': edge_weight, 'node_vec1': node_vec1, 'L0_gnn_W_self': _L0_gnn_in['W_self'], 'L0_gnn_b_self': _L0_gnn_in['b_self'], 'L0_gnn_W_neigh': _L0_gnn_in['W_neigh'], 'L0_gnn_b_neigh': _L0_gnn_in['b_neigh'], 'L0_gnn_scale': _L0_gnn_in['scale'], 'L0_gnn_offset': _L0_gnn_in['offset'], 'L1_gnn_W_sc0': _L1_gnn_in['W_sc0'], 'L1_gnn_W_sc1': _L1_gnn_in['W_sc1'], 'L1_gnn_W_l1_0': _L1_gnn_in['W_l1_0'], 'L1_gnn_W_l1_1': _L1_gnn_in['W_l1_1'], 'L1_gnn_W_fc1': _L1_gnn_in['W_fc1'], 'L1_gnn_W_fc2': _L1_gnn_in['W_fc2'], 'L1_gnn_W_l2_A0': _L1_gnn_in['W_l2_A0'], 'L1_gnn_W_l2_B0': _L1_gnn_in['W_l2_B0'], 'L1_gnn_W_l2_C1': _L1_gnn_in['W_l2_C1'], 'L1_gnn_W_l2_D1': _L1_gnn_in['W_l2_D1'], 'L1_gnn_W_l3_A': _L1_gnn_in['W_l3_A'], 'L1_gnn_W_l3_B': _L1_gnn_in['W_l3_B']}

def reference(x, src, dst, edge_attr_4, edge_attr_64, edge_weight, node_vec1, L0_gnn_W_self, L0_gnn_b_self, L0_gnn_W_neigh, L0_gnn_b_neigh, L0_gnn_scale, L0_gnn_offset, L1_gnn_W_sc0, L1_gnn_W_sc1, L1_gnn_W_l1_0, L1_gnn_W_l1_1, L1_gnn_W_fc1, L1_gnn_W_fc2, L1_gnn_W_l2_A0, L1_gnn_W_l2_B0, L1_gnn_W_l2_C1, L1_gnn_W_l2_D1, L1_gnn_W_l3_A, L1_gnn_W_l3_B):
    import jax
    import jax.numpy as jnp

    def _L0_gnn_ref(feat_in, edge_row, edge_col, edge_val, W_self, b_self, W_neigh, b_neigh, scale, offset):
        import jax, jax.numpy as jnp
        import numpy as np
        N_NODES = 6250
        N_EDGES = 100000
        DIM_IN = 128
        DIM_OUT = 128
        EPS = 1e-09

        def _branch(x, W, b, scale, offset, idx):
            h = jax.nn.relu(x @ W.T + b)
            mean = jnp.mean(h, axis=1, keepdims=True)
            var = jnp.var(h, axis=1, keepdims=True) + EPS
            d = h.shape[1]
            s = scale[idx * d:(idx + 1) * d]
            o = offset[idx * d:(idx + 1) * d]
            return (h - mean) * s * jax.lax.rsqrt(var) + o
        n = feat_in.shape[0]
        feat_neigh = jax.ops.segment_sum(edge_val[:, None] * feat_in[edge_col], edge_row, num_segments=n)
        feat_self_trans = _branch(feat_in, W_self, b_self, scale, offset, 0)
        feat_neigh_trans = _branch(feat_neigh, W_neigh, b_neigh, scale, offset, 1)
        return feat_self_trans + feat_neigh_trans

    def _L1_gnn_ref(node_input, node_attr, edge_src, edge_dst, edge_attr, edge_scalars, W_sc0, W_sc1, W_l1_0, W_l1_1, W_fc1, W_fc2, W_l2_A0, W_l2_B0, W_l2_C1, W_l2_D1, W_l3_A, W_l3_B):
        import jax, jax.numpy as jnp
        import numpy as np
        MUL = 32
        N_NODES = 6250
        N_EDGES = 100000
        NUM_NEIGHBORS = 16.0
        SQRT3 = 3.0 ** 0.5
        SILU_NORM = 1.679

        def split_irreps(x):
            x0 = x[..., :MUL]
            x1 = x[..., MUL:].reshape(x.shape[:-1] + (MUL, 3))
            return (x0, x1)

        def merge_irreps(x0, x1):
            return jnp.concatenate([x0, x1.reshape(x1.shape[:-2] + (MUL * 3,))], axis=-1)

        def fctp_scalar(x0, x1, a, W0, W1, fan_in):
            s = a / jnp.sqrt(jnp.asarray(fan_in, x0.dtype))
            o0 = x0 @ W0 * s
            o1 = jnp.einsum('nud,uw->nwd', x1, W1) * s[..., None]
            return (o0, o1)
        n = node_input.shape[0]
        x0, x1 = split_irreps(node_input)
        h = SILU_NORM * jax.nn.silu(edge_scalars @ (W_fc1 / 8.0))
        weight = h @ (W_fc2 / 8.0)
        sc0, sc1 = fctp_scalar(x0, x1, node_attr, W_sc0, W_sc1, MUL)
        f0, f1 = fctp_scalar(x0, x1, node_attr, W_l1_0, W_l1_1, MUL)
        g0 = f0[edge_src]
        g1 = f1[edge_src]
        e0 = edge_attr[:, :1]
        e1 = edge_attr[:, 1:]
        wA, wC, wD, wB = (weight[:, :MUL], weight[:, MUL:2 * MUL], weight[:, 2 * MUL:3 * MUL], weight[:, 3 * MUL:])
        outA = wA * g0 * e0
        outB = wB * jnp.einsum('euk,ek->eu', g1, e1) / SQRT3
        outC = (wC * g0)[..., None] * e1[:, None, :]
        outD = wD[..., None] * g1 * e0[..., None]
        seg = lambda v: jax.ops.segment_sum(v, edge_dst, num_segments=n)
        inv = 1.0 / jnp.sqrt(jnp.asarray(NUM_NEIGHBORS, node_input.dtype))
        mA, mB, mC, mD = (seg(outA) * inv, seg(outB) * inv, seg(outC) * inv, seg(outD) * inv)
        s = node_attr / 8.0
        c0 = (mA @ W_l2_A0 + mB @ W_l2_B0) * s
        c1 = (jnp.einsum('nud,uw->nwd', mC, W_l2_C1) + jnp.einsum('nud,uw->nwd', mD, W_l2_D1)) * s[..., None]
        angle = 0.1 * (mA @ W_l3_A + mB @ W_l3_B) * s
        cos, sin = (jnp.cos(angle), jnp.sin(angle))
        return cos * merge_irreps(sc0, sc1) + sin * merge_irreps(c0, c1)
    x = _layernorm(x + _L0_gnn_ref(x, src, dst, edge_weight, L0_gnn_W_self, L0_gnn_b_self, L0_gnn_W_neigh, L0_gnn_b_neigh, L0_gnn_scale, L0_gnn_offset), axis=-1)
    x = _layernorm(x + _L1_gnn_ref(x, node_vec1, src, dst, edge_attr_4, edge_attr_64, L1_gnn_W_sc0, L1_gnn_W_sc1, L1_gnn_W_l1_0, L1_gnn_W_l1_1, L1_gnn_W_fc1, L1_gnn_W_fc2, L1_gnn_W_l2_A0, L1_gnn_W_l2_B0, L1_gnn_W_l2_C1, L1_gnn_W_l2_D1, L1_gnn_W_l3_A, L1_gnn_W_l3_B), axis=-1)
    return x

_drawn_inputs = setup_inputs


def setup_inputs(seed=0):
    import zlib

    import numpy as np

    out = dict(_drawn_inputs(seed))
    spreads = {'L0_gnn_scale': (1.0, 0.2), 'L0_gnn_offset': (0.0, 0.1)}
    factors = {'edge_attr_4': 5.675,
     'edge_attr_64': 5.66,
     'L0_gnn_b_self': 6.786,
     'L0_gnn_b_neigh': 8.0,
     'L1_gnn_W_l1_0': 6.813,
     'L1_gnn_W_l1_1': 6.144,
     'L1_gnn_W_fc1': 5.641,
     'L1_gnn_W_fc2': 5.568,
     'L1_gnn_W_l2_A0': 8.0,
     'L1_gnn_W_l2_B0': 8.0,
     'L1_gnn_W_l2_C1': 8.0,
     'L1_gnn_W_l2_D1': 8.0,
     'L1_gnn_W_l3_A': 8.0,
     'L1_gnn_W_l3_B': 6.041,
     'L1_gnn_W_sc0': 64.0,
     'L1_gnn_W_sc1': 52.307}
    for name, (base, spread) in spreads.items():
        noise = np.random.default_rng([zlib.crc32(name.encode()), seed]).standard_normal(out[name].shape)
        drawn = base * np.exp(spread * noise) if base else spread * noise
        out[name] = jnp.asarray(drawn.astype(out[name].dtype))
    for name, factor in factors.items():
        out[name] = (out[name] * factor).astype(out[name].dtype)
    return out
```

```python
import concourse.bass as bass
from concourse import mybir
from contextlib import ExitStack

F32 = mybir.dt.float32
I32 = mybir.dt.int32
ALU = mybir.AluOpType
ACT = mybir.ActivationFunctionType
AX = mybir.AxisListType

P = 128
N = 12500
E = 200000
D = 128
MUL = 32
EF = 64
TH = 4
HE = P * TH
TS = 2 * TH
SG = 2 * HE
NSG = -(-E // SG)
NFULL = E // SG
LAST = E - SG
TWICE = NFULL * SG - LAST
NH = 2 * NSG
W = 40
NT = N + W + 4
FAR = 1.0e6
NP = 125
CB = 4
NB = N // (NP * CB)
BN = NP * CB
ROUND = 12582912.0
PI = 3.14159250
TWO_PI = (6.28125, 1.9340515136718750e-3, 1.2556635e-6)
NTAB = 4
NPAD = 99 * P
UN = 4


def sweep(eng, body, first, last, lo, hi):
    for s in range(first, lo):
        body(s, s // UN, s % UN)
    with eng.Fori(lo // UN, hi // UN) as q:
        for j in range(UN):
            body(q * UN + j, q, j)
    for s in range(hi, last):
        body(s, s // UN, s % UN)


def at(s, q, j, back):
    return s - back, q + (j - back) // UN, (j - back) % UN


def settle(eng, mark):
    eng.sem_inc(mark, 1)


def done(eng, signal, step, back=0):
    if not isinstance(step, int) or step >= back:
        eng.wait_ge(signal, step - back + 1)


def uses(eng, signal, rnd, each):
    if not isinstance(rnd, int) or rnd > 0:
        eng.wait_ge(signal, rnd * each)


def refine(dve, v, r0, t, r, steps, m):
    dve.scalar_tensor_tensor(out=t[:, 0, :], in0=r0, scalar=-0.5, in1=v, op0=ALU.mult, op1=ALU.mult).then_inc(steps, 1)
    dve.wait_ge(steps, m * 3 + 1)
    dve.tensor_tensor(t[:, 1, :], t[:, 0, :], r0, ALU.mult).then_inc(steps, 1)
    dve.wait_ge(steps, m * 3 + 2)
    dve.scalar_tensor_tensor(out=r, in0=t[:, 1, :], scalar=1.5, in1=r0, op0=ALU.add, op1=ALU.mult).then_inc(steps, 1)
    dve.wait_ge(steps, m * 3 + 3)


def graph_layers(nc, a, out):
    with ExitStack() as ctx:
        def sb(name, shape, dt=F32):
            return ctx.enter_context(nc.sbuf_tensor(name, shape, dt))

        def sem(name):
            return ctx.enter_context(nc.semaphore(name))

        def bank(name, shape, scope):
            return scope.enter_context(nc.psum_tensor(name, shape, F32))

        base_d = nc.dram_tensor("base_scratch", (N, D), F32, kind="Internal").ap()
        f_d = nc.dram_tensor("f_scratch", (N, D), F32, kind="Internal").ap()
        xs_d = nc.dram_tensor("xs_scratch", (N, 2 * D), F32, kind="Internal").ap()
        passed = sem("passed")
        sums_d = [nc.dram_tensor(f"sums_scratch{i}", (NPAD, D), F32, kind="Internal").ap() for i in range(NTAB)]
        ang_d = nc.dram_tensor("angle_scratch", (1, N), F32, kind="Internal").ap()

        table = sb("table", [P, 2, NT])
        dstf = sb("dstf", [P, NH, TH])
        dst0 = sb("dst0", [P, NH, TH])
        base0 = sb("base0", [P, NH])
        base = sb("base", [P, NH])
        base_i = sb("base_i", [1, NH], I32)
        near0 = sb("near0", [P, NH])
        near_i = sb("near_i", [1, NH], I32)
        lower = sb("lower", [P, P])
        spare = sb("spare", [P, 1])
        npass_i = sb("npass_i", [1, 1], I32)
        iota_f = sb("iota_f", [P, P])
        ident = sb("ident", [P, P])
        ones = sb("ones", [P, P])
        self_wT = sb("self_wT", [P, D])
        neigh_wT = sb("neigh_wT", [P, D])
        node_w = sb("node_w", [P, 2 * D])
        fc1_w = sb("fc1_w", [P, 2 * EF])
        fc2_w = sb("fc2_w", [P, 2 * D])
        lin_w = sb("lin_w", [P, 5, D])
        bias4 = sb("bias4", [1, 2, CB, D])
        vecs = sb("vecs", [P, 4, D])
        attr = sb("attr", [NP, NB * CB])
        attr_s = sb("attr_s", [NP, NB * CB])

        with ExitStack() as s0:
            def tmp(name, shape, dt=F32):
                return s0.enter_context(nc.sbuf_tensor(name, shape, dt))
            dst_i = tmp("dst_i", [P, NH, TH], I32)
            iota_i = tmp("iota_i", [P, P], I32)
            part_i = tmp("part_i", [P, 1], I32)
            part_f = tmp("part_f", [P, 1])
            w_nat = tmp("w_nat", [P, 2, D])
            sc_f = tmp("sc_f", [P, D])
            lin_f = tmp("lin_f", [P, 4, D])
            ang_f = tmp("ang_f", [P, 1])
            rows = tmp("rows", [1, 4, D])
            brow = tmp("brow", [1, 2, D])
            attr_r = tmp("attr_r", [NB * CB, NP])
            lo_p = tmp("lo_p", [P, NH])
            hi_p = tmp("hi_p", [P, NH])
            last_m = tmp("last_m", [P, 2, TH])
            ext = tmp("ext", [98, 2, 4])
            diag = tmp("diag", [98, 4, 98])
            span = tmp("span", [98, 4])
            span1 = tmp("span1", [98, 1])
            tot = tmp("tot", [1, 4])
            base_c = tmp("base_c", [1, NH])
            ps_w = bank("ps_w", [P, 2, D], s0)
            ps_at = bank("ps_at", [NP, NB * CB], s0)
            ps_lo = bank("ps_lo", [98, 4, P], s0)
            ps_hi = bank("ps_hi", [98, 4, P], s0)
            ps_b = bank("ps_b", [P, NH], s0)
            ps_v = bank("ps_v", [P, 4, D], s0)
            ps_s = bank("ps_s", [1, 98], s0)
            zeroed, idn, idf = sem("zeroed"), sem("idn"), sem("idf")
            dst_in, dst2_in, wts_in, blk_in = sem("dst_in"), sem("dst2_in"), sem("wts_in"), sem("blk_in")
            ext_p, ext_t, ext_d, diag_d, bc_d = sem("ext_p"), sem("ext_t"), sem("ext_d"), sem("diag_d"), sem("bc_d")
            span_d, span_t = sem("span_d"), sem("span_t")
            wT_d, step0 = sem("wT_d"), sem("step0")
            NCH = NH // 98
            assert NH == 98 * 4

            with nc.Block() as block:
                @block.sync
                def _(sp):
                    full = a["dst"][0:NFULL * SG].rearrange("(s h p k) -> p (s h) k", h=2, p=P, k=TH)
                    sp.dma_start(dst_i[:, 0:2 * NFULL, :], full).then_inc(dst_in, 16)
                    sp.dma_start(dst_i[:, 2 * NFULL:NH, :],
                                 a["dst"][LAST:E].rearrange("(h p k) -> p h k", h=2, p=P)).then_inc(dst2_in, 16)
                    sp.dma_start(w_nat[:, 0, :], a["L0_gnn_W_self"]).then_inc(wts_in, 16)
                    sp.dma_start(w_nat[:, 1, :], a["L0_gnn_W_neigh"]).then_inc(wts_in, 16)
                    sp.dma_start(rows[:, 0:2, :], a["L0_gnn_scale"].rearrange("(o b d) -> o b d", o=1, b=2)).then_inc(wts_in, 16)
                    sp.dma_start(rows[:, 2:4, :], a["L0_gnn_offset"].rearrange("(o b d) -> o b d", o=1, b=2)).then_inc(wts_in, 16)
                    sp.dma_start(brow[:, 0, :], a["L0_gnn_b_self"].rearrange("(o d) -> o d", o=1)).then_inc(wts_in, 16)
                    sp.dma_start(brow[:, 1, :], a["L0_gnn_b_neigh"].rearrange("(o d) -> o d", o=1)).then_inc(wts_in, 16)
                    sp.dma_start(attr_r[:, :], a["node_vec1"].rearrange("(t p) o -> t (p o)", p=NP)).then_inc(wts_in, 16)

                @block.scalar
                def _(act):
                    act.wait_ge(zeroed, 5)
                    n = 0

                    def put(to, fro):
                        nonlocal n
                        act.dma_start(to, fro).then_inc(blk_in, 16)
                        n += 16
                    for r in range(2):
                        put(fc1_w[EF * r:EF * (r + 1), EF * r:EF * (r + 1)], a["L1_gnn_W_fc1"])
                        put(fc2_w[EF * r:EF * (r + 1), D * r:D * (r + 1)], a["L1_gnn_W_fc2"])
                    put(node_w[0:MUL, D:D + MUL], a["L1_gnn_W_l1_0"])
                    put(sc_f[0:MUL, 0:MUL], a["L1_gnn_W_sc0"])
                    put(lin_f[0:MUL, 0, 0:MUL], a["L1_gnn_W_l2_A0"])
                    put(ang_f[0:MUL, 0:1], a["L1_gnn_W_l3_A"])
                    for d in range(3):
                        c = MUL * (d + 1)
                        put(node_w[MUL + d:D:3, D + c:D + c + MUL], a["L1_gnn_W_l1_1"])
                        put(sc_f[MUL + d:D:3, c:c + MUL], a["L1_gnn_W_sc1"])
                        put(lin_f[c:c + MUL, 0, c:c + MUL], a["L1_gnn_W_l2_D1"])
                        put(lin_f[0:MUL, d + 1, c:c + MUL], a["L1_gnn_W_l2_C1"])
                        put(lin_f[c:c + MUL, d + 1, 0:MUL], a["L1_gnn_W_l2_B0"])
                        put(ang_f[c:c + MUL, 0:1], a["L1_gnn_W_l3_B"])
                    assert n == 16 * 26

                @block.gpsimd
                def _(pool):
                    pool.memset(fc1_w[:, :], 0.0).then_inc(zeroed, 1)
                    pool.memset(fc2_w[:, :], 0.0).then_inc(zeroed, 1)
                    pool.memset(node_w[:, :], 0.0).then_inc(zeroed, 1)
                    pool.memset(sc_f[:, :], 0.0).then_inc(zeroed, 1)
                    pool.memset(ident[:, :], 0.0).then_inc(idn, 1)
                    pool.iota(iota_i[:, :], pattern=[[1, P]], base=0, channel_multiplier=0).then_inc(idn, 1)
                    pool.iota(part_i[:, :], pattern=[[1, 1]], base=0, channel_multiplier=1).then_inc(idn, 1)
                    pool.memset(ones[:, :], 1.0).then_inc(idn, 1)
                    pool.wait_ge(idn, 1)
                    pool.affine_select(out=ident[:, :], in_=ident[:, :], compare_op=ALU.not_equal, fill=1.0,
                                       base=0, pattern=[[-1, P]], channel_multiplier=1).then_inc(idf, 1)
                    pool.memset(table[:, 1, :], 0.0).then_inc(idf, 1)

                @block.vector
                def _(dve):
                    step = 0

                    def link(ins):
                        nonlocal step
                        step += 1
                        ins.then_inc(step0, 1)
                        dve.wait_ge(step0, step)
                    dve.memset(lin_f[:, :, :], 0.0).then_inc(zeroed, 1)
                    dve.memset(table[:, 0, :], 0.0)
                    dve.wait_ge(dst2_in, 16)
                    dve.wait_ge(dst_in, 16)
                    link(dve.tensor_copy(dstf[:, :, :], dst_i[:, :, :]))
                    t0 = TWICE // HE
                    link(dve.memset(dstf[:, 2 * NFULL:2 * NFULL + t0, :], FAR))
                    link(dve.memset(dstf[0:(TWICE - t0 * HE) // TH, 2 * NFULL + t0, :], FAR))
                    dve.tensor_reduce(lo_p[:, :], dstf[:, :, :], AX.X, ALU.min)
                    link(dve.tensor_scalar(last_m[:, :, :], dstf[:, 2 * NFULL:NH, :], FAR, None, ALU.is_lt))
                    link(dve.tensor_tensor(last_m[:, :, :], last_m[:, :, :], dstf[:, 2 * NFULL:NH, :], ALU.mult))
                    dve.tensor_reduce(hi_p[:, 0:2 * NFULL], dstf[:, 0:2 * NFULL, :], AX.X, ALU.max)
                    dve.tensor_reduce(hi_p[:, 2 * NFULL:NH], last_m[:, :, :], AX.X, ALU.max).then_inc(ext_p, 1)
                    dve.wait_ge(idn, 4)
                    dve.tensor_copy(iota_f[:, :], iota_i[:, :])
                    link(dve.tensor_copy(part_f[:, :], part_i[:, :]))
                    dve.tensor_scalar(lower[:, :], iota_f[:, :], part_f[:, 0:1], None, ALU.is_lt)
                    dve.tensor_scalar(spare[:, :], part_f[:, :], float(N), None, ALU.add)
                    dve.tensor_copy(dst0[:, :, :], dstf[:, :, :])
                    dve.wait_ge(ext_t, 1)
                    dve.tensor_reduce(ext[:, 0, :], ps_lo[:, :, :], AX.X, ALU.min)
                    link(dve.tensor_reduce(ext[:, 1, :], ps_hi[:, :, :], AX.X, ALU.max))
                    link(dve.tensor_tensor(span[:, :], ext[:, 1, :], ext[:, 0, :], ALU.subtract))
                    dve.tensor_tensor(diag[:, :, :], ident[0:98, None, 0:98].to_broadcast([98, 4, 98]),
                                      ext[:, 0, :, None].to_broadcast([98, 4, 98]), ALU.mult).then_inc(diag_d, 1)
                    link(dve.tensor_reduce(span1[:, :], span[:, :], AX.X, ALU.max))
                    dve.wait_ge(wts_in, 16 * 7)
                    dve.tensor_copy(bias4[:, :, :, :], brow[:, :, None, :].to_broadcast([1, 2, CB, D])).then_inc(span_d, 1)
                    dve.wait_ge(span_t, 1)
                    link(dve.tensor_reduce(tot[:, 0:1], ps_s[:, :], AX.X, ALU.max))
                    link(dve.tensor_scalar(tot[:, 1:2], tot[:, 0:1], 1.0 / W, 0.5 + 0.25 / W, ALU.mult, ALU.add))
                    link(dve.tensor_scalar(tot[:, 2:3], tot[:, 1:2], ROUND, ROUND, ALU.add, ALU.subtract))
                    dve.tensor_copy(npass_i[:, :], tot[:, 2:3])
                    dve.wait_ge(bc_d, 1)
                    link(dve.tensor_scalar(base0[:, :], ps_b[:, :], float(N), None, ALU.min))
                    dve.tensor_copy(base[:, :], base0[:, :])
                    dve.tensor_copy(base_i[:, :], base0[0:1, :])
                    link(dve.tensor_scalar(near0[:, :], base0[:, :], float(N - W), None, ALU.min))
                    dve.tensor_copy(near_i[:, :], near0[0:1, :])
                    dve.wait_ge(wT_d, 1)
                    dve.tensor_copy(self_wT[:, :], ps_w[:, 0, :])
                    dve.tensor_copy(neigh_wT[:, :], ps_w[:, 1, :])
                    dve.tensor_copy(vecs[:, :, :], ps_v[:, :, :])
                    link(dve.tensor_copy(attr[:, :], ps_at[:, :]))
                    dve.tensor_scalar(attr_s[:, :], attr[:, :], float(MUL) ** -0.5, None, ALU.mult)
                    dve.wait_ge(blk_in, 16 * 26)
                    for d in range(3):
                        c = MUL * (d + 1)
                        dve.tensor_scalar(lin_f[c:c + MUL, d + 1, 0:MUL], lin_f[c:c + MUL, d + 1, 0:MUL],
                                          3.0 ** -0.5, None, ALU.mult)
                        dve.tensor_scalar(ang_f[c:c + MUL, 0:1], ang_f[c:c + MUL, 0:1],
                                          3.0 ** -0.5, None, ALU.mult)
                    dve.tensor_scalar(fc1_w[:, :], fc1_w[:, :], 1.0 / 8.0, None, ALU.mult)
                    link(dve.tensor_scalar(fc2_w[:, :], fc2_w[:, :], 1.0 / 8.0, None, ALU.mult))
                    dve.tensor_copy(node_w[:, 0:MUL], sc_f[:, 0:MUL])
                    dve.tensor_copy(node_w[:, MUL:D].rearrange("p (w d) -> p d w", d=3),
                                    sc_f[:, MUL:D].rearrange("p (d w) -> p d w", d=3))
                    dve.tensor_copy(lin_w[:, 4, :], ang_f[:, 0:1].to_broadcast([P, D]))
                    dve.tensor_copy(lin_w[:, 0:4, 0:MUL], lin_f[:, :, 0:MUL])
                    dve.tensor_copy(lin_w[:, 0:4, MUL:D].rearrange("p k (w d) -> p k d w", d=3),
                                    lin_f[:, :, MUL:D].rearrange("p k (d w) -> p k d w", d=3))

                @block.tensor
                def _(pe):
                    pe.wait_ge(idf, 1)
                    pe.wait_ge(idn, 4)
                    pe.wait_ge(wts_in, 16 * 7)
                    for r in range(2):
                        pe.transpose(ps_w[:, r, :], w_nat[:, r, :], ident[:, :])
                    pe.transpose(ps_at[:, :], attr_r[:, :], ident[0:NB * CB, 0:NB * CB])
                    pe.matmul(ps_v[:, :, :], ones[0:1, :], rows[:, :, :], start=True, stop=True).then_inc(wT_d, 1)
                    pe.wait_ge(ext_p, 1)
                    for c in range(4):
                        pe.transpose(ps_lo[:, c, :], lo_p[:, 98 * c:98 * (c + 1)], ident[:, :])
                        last = pe.transpose(ps_hi[:, c, :], hi_p[:, 98 * c:98 * (c + 1)], ident[:, :])
                    last.then_inc(ext_t, 1)
                    pe.wait_ge(diag_d, 1)
                    pe.matmul(ps_b[:, :], ones[0:98, :], diag[:, :, :], start=True, stop=True).then_inc(bc_d, 1)
                    pe.wait_ge(span_d, 1)
                    pe.transpose(ps_s[:, :], span1[:, :], ident[0:98, 0:98]).then_inc(span_t, 1)

        def rows_of(t, b):
            return t[bass.ds(b * BN, BN), :].rearrange("(c p) d -> p c d", p=NP)

        def live(b):
            return not isinstance(b, int) or 0 <= b < NB

        with ExitStack() as s1:
            def tmp(name, shape, dt=F32):
                return s1.enter_context(nc.sbuf_tensor(name, shape, dt))
            x_in = tmp("x_in", [NP, UN, CB, D])
            xT = tmp("xT", [P, 2, CB, NP])
            h = tmp("h_s", [NP, 2, CB, D])
            hn = tmp("hn_s", [NP, 2, CB, D])
            res = tmp("res_s", [NP, UN, CB, D])
            offs = tmp("offs_s", [NP, D])
            st6 = tmp("st6_s", [NP, CB, 6])
            mv = tmp("mv_s", [NP, 2, CB, 2])
            var = tmp("var_s", [NP, 2, CB])
            sd = tmp("sd_s", [NP, 2, CB])
            r0 = tmp("r0_s", [NP, CB])
            nw = tmp("nw_s", [NP, 2, CB])
            rs = tmp("rs_s", [NP, CB])
            ps_t = [bank(f"ps_st{i}", [P, CB, P], s1) for i in range(2)]
            ps_m = [bank(f"ps_sm{i}", [NP, CB, D], s1) for i in range(2)]
            x_ld = [sem(f"self_x_ld{i}") for i in range(UN)]
            res_st = [sem(f"self_res_st{i}") for i in range(UN)]
            s_tr, s_xT, s_mm, s_relu = sem("self_tr"), sem("self_xT"), sem("self_mm"), sem("self_relu")
            s_stat, s_agg, s_var, s_sd = sem("self_stat"), sem("self_agg"), sem("self_var"), sem("self_sd")
            s_rs, s_cen, s_hn, s_add, s_res = sem("self_rs"), sem("self_cen"), sem("self_hn"), sem("self_add"), sem("self_res")
            s_nw = sem("self_nw")
            s_off, z_st = sem("self_off"), sem("sums_zeroed")

            with nc.Block() as block:
                @block.sync
                def _(sp):
                    def body(b, q, j):
                        if live(b):
                            done(sp, s_res, b, UN)
                            sp.dma_start(x_in[:, j, :, :], rows_of(a["x"], b)).then_inc(x_ld[j], 16)
                        m, r, i = at(b, q, j, 3)
                        if live(m):
                            done(sp, s_res, m)
                            sp.dma_start(rows_of(base_d, m), res[:, i, :, :]).then_inc(res_st[i], 16)
                    sweep(sp, body, 0, NB + 3, 4, 24)
                    for i in range(UN):
                        sp.wait_ge(res_st[i], 16 * len(range(i, NB, UN)))

                @block.tensor
                def _(pe):
                    def body(b, q, j):
                        if live(b):
                            uses(pe, x_ld[j], q + 1, 16)
                            done(pe, s_xT, b, 2)
                            for c in range(CB):
                                last = pe.transpose(ps_t[j % 2][:, c, 0:NP], x_in[:, j, c, :], ident[0:NP, 0:NP])
                            last.then_inc(s_tr, 1)
                        m, r, i = at(b, q, j, 1)
                        if live(m):
                            k = i % 2
                            done(pe, s_xT, m)
                            done(pe, s_relu, m, 2)
                            pe.matmul(ps_m[k][:, :, :], ones[0:1, 0:NP], bias4[:, 0, :, :], start=True, stop=False,
                                      skip_group_check=True)
                            for c in range(CB):
                                last = pe.matmul(ps_m[k][:, c, :], xT[:, k, c, :], self_wT[:, :], start=False,
                                                 stop=(c == CB - 1), skip_group_check=True)
                            last.then_inc(s_mm, 1)
                    sweep(pe, body, 0, NB + 1, 4, 24)

                @block.scalar
                def _(act):
                    ZPART = NPAD * D // P // (24 // UN)
                    assert NTAB == UN and ZPART * (24 // UN) * P == NPAD * D

                    def body(b, q, j):
                        if not isinstance(b, int) or b < 24:
                            act.dma_start(sums_d[j].rearrange("(p r) d -> p (r d)", p=P)[:, bass.ds(q * ZPART, ZPART)],
                                          table[:, 0, 0:ZPART]).then_inc(z_st, 16)
                        if live(b):
                            done(act, s_tr, b)
                            done(act, s_mm, b, 2)
                            act.copy(xT[:, j % 2, :, :], ps_t[j % 2][:, :, 0:NP]).then_inc(s_xT, 1)
                        m, r, i = at(b, q, j, 2)
                        if live(m):
                            done(act, s_var, m)
                            done(act, s_rs, m, 2)
                            act.activation(sd[:, i % 2, :], var[:, i % 2, :], ACT.Sqrt).then_inc(s_sd, 1)
                        m, r, i = at(b, q, j, 1)
                        if live(m):
                            done(act, s_mm, m)
                            done(act, s_cen, m, 2)
                            act.activation(h[:, i % 2, :, :], ps_m[i % 2][:, :, :], ACT.Relu).then_inc(s_relu, 1)
                    sweep(act, body, 0, NB + 2, 4, 24)
                    act.wait_ge(z_st, 16 * 24)

                @block.vector
                def _(dve):
                    dve.tensor_tensor(offs[:, :], vecs[0:NP, 2, :], vecs[0:NP, 3, :], ALU.add).then_inc(s_off, 1)

                    def body(b, q, j):
                        m, r, i = at(b, q, j, 1)
                        if live(m):
                            k = i % 2
                            done(dve, s_relu, m)
                            for c in range(CB):
                                last = dve.bn_stats(st6[:, c, :], h[:, k, c, :])
                            last.then_inc(s_stat, 1)
                            done(dve, s_stat, m)
                            settle(dve, passed)
                            for c in range(CB):
                                last = dve.bn_aggr(mv[:, k, c, :], st6[:, c, :])
                            last.then_inc(s_agg, 1)
                            done(dve, s_agg, m)
                            done(dve, s_sd, m, 2)
                            dve.tensor_scalar(var[:, k, :], mv[:, k, :, 1], 1e-9, None, ALU.add).then_inc(s_var, 1)
                        m, r, i = at(b, q, j, 2)
                        if live(m):
                            k = i % 2
                            done(dve, s_sd, m)
                            done(dve, s_cen, m, 1)
                            dve.reciprocal(r0[:, :], sd[:, k, :]).then_inc(s_rs, 1)
                            done(dve, s_rs, m)
                            refine(dve, var[:, k, :], r0[:, :], nw, rs[:, :], s_nw, m)
                            done(dve, s_add, m, 2)
                            for c in range(CB):
                                last = dve.tensor_scalar(hn[:, k, c, :], h[:, k, c, :], mv[:, k, c, 0:1], rs[:, c:c + 1],
                                                         ALU.subtract, ALU.mult)
                            last.then_inc(s_cen, 1)
                            done(dve, s_cen, m)
                            dve.tensor_tensor(hn[:, k, :, :], hn[:, k, :, :],
                                              vecs[0:NP, 0, None, :].to_broadcast([NP, CB, D]), ALU.mult).then_inc(s_hn, 1)
                    sweep(dve, body, 0, NB + 2, 4, 24)

                @block.gpsimd
                def _(pool):
                    pool.wait_ge(s_off, 1)

                    def body(b, q, j):
                        m, r, i = at(b, q, j, 2)
                        if live(m):
                            done(pool, s_hn, m)
                            uses(pool, res_st[i], r, 16)
                            pool.tensor_tensor(res[:, i, :, :], hn[:, i % 2, :, :], x_in[:, i, :, :], ALU.add).then_inc(s_add, 1)
                            done(pool, s_add, m)
                            pool.tensor_tensor(res[:, i, :, :], res[:, i, :, :],
                                               offs[:, None, :].to_broadcast([NP, CB, D]), ALU.add).then_inc(s_res, 1)
                    sweep(pool, body, 0, NB + 2, 4, 24)

        def first_edge(eng, s):
            return min(s * SG, LAST) if isinstance(s, int) else eng.snap(s * SG)

        def edges_of(t, e0, tail):
            v = t[bass.ds(e0, SG)]
            return v.rearrange("(h p k) -> p h k", h=2, p=P) if not tail else \
                v.rearrange("(h p k) e -> p h (k e)", h=2, p=P)

        def live_sg(s):
            return not isinstance(s, int) or 0 <= s < NSG

        with ExitStack() as s2:
            def tmp(name, shape, dt=F32):
                return s2.enter_context(nc.sbuf_tensor(name, shape, dt))

            def sem(name):
                return s2.enter_context(nc.semaphore(name))
            src_s = tmp("src_s", [P, UN, TS], I32)
            srow_s = tmp("srow_s", [P, UN, SG], I32)
            ew_s = tmp("ew_s", [P, UN, TS])
            xw_s = tmp("xw_s", [W, UN, 2, D])
            srcf = tmp("srcf", [P, TS])
            rel = tmp("rel0", [P, 2, TH])
            hot = tmp("hot0", [P, 2, TS, W])
            same = tmp("same", [P, 2, TS, P])
            junk = tmp("junk", [P, TS, P])
            before = tmp("before", [P, TS])
            away = tmp("away", [P, 2, TS])
            to_i = tmp("to_i", [P, UN, TS], I32)
            near = tmp("near", [W, 2, TS, P])
            vals = tmp("vals", [P, UN, TS, D])
            past = tmp("past", [P, NH, TH])
            ps_n = [bank(f"ps_n{i}", [W, TH, P], s2) for i in range(4)]
            ps_v = [bank(f"ps_v{i}", [P, TH, D], s2) for i in range(4)]
            ld = [sem(f"n_ld{i}") for i in range(UN)]
            xw_ld = [sem(f"n_xw_ld{i}") for i in range(UN)]
            added = [sem(f"n_added{i}") for i in range(NTAB)]
            n_srcf, n_rel, n_hot, n_same, n_before = sem("n_srcf"), sem("n_rel"), sem("n_hot"), sem("n_same"), sem("n_before")
            n_away, n_away2, n_to, n_psn, n_near = sem("n_away"), sem("n_away2"), sem("n_to"), sem("n_psn"), sem("n_near")
            n_psv, n_vals, n_scat, n_bases = sem("n_psv"), sem("n_vals"), sem("n_scat"), sem("n_bases")
            sems0 = ld + xw_ld + added + [n_srcf, n_rel, n_hot, n_same, n_before, n_away, n_away2, n_to, n_psn, n_near,
                                          n_psv, n_vals, n_scat, n_bases]
            PER = TS // NTAB

            npass = nc.values_load(npass_i[0:1, 0:1], min_val=1, max_val=N // W + 1)
            with nc.Fori(0, npass):
                with nc.Block() as block:
                    @block.sync
                    def _(sp):
                        def body(s, q, j):
                            b0 = sp.value_load(near_i[0:1, bass.ds(s * 2, 1)], min_val=0, max_val=N - W)
                            b1 = sp.value_load(near_i[0:1, bass.ds(s * 2 + 1, 1)], min_val=0, max_val=N - W)
                            e0 = first_edge(sp, s)
                            done(sp, n_to, s, UN)
                            settle(sp, passed)
                            done(sp, n_psv, s, UN)
                            settle(sp, passed)
                            sp.dma_start(src_s[:, j, :].rearrange("p (h k) -> p h k", h=2),
                                         edges_of(a["src"], e0, False)).then_inc(ld[j], 16)
                            sp.dma_start(srow_s[:, j, :],
                                         a["src"][bass.ds(e0, SG)].rearrange("(o e) -> o e", o=1).to_broadcast([P, SG])).then_inc(ld[j], 16)
                            sp.dma_start(ew_s[:, j, :].rearrange("p (h k) -> p h k", h=2),
                                         edges_of(a["edge_weight"], e0, False)).then_inc(ld[j], 16)
                            sp.dma_start(xw_s[:, j, 0, :], a["x"][bass.ds(b0, W), :]).then_inc(xw_ld[j], 16)
                            sp.dma_start(xw_s[:, j, 1, :], a["x"][bass.ds(b1, W), :]).then_inc(xw_ld[j], 16)
                        sweep(sp, body, 0, NSG, 4, 192)

                    @block.vector
                    def _(dve):
                        def body(s, q, j):
                            k = j % 2
                            rows = srow_s[:, j, :].rearrange("p (h e k) -> p h k e", h=2, k=TH)
                            uses(dve, ld[j], q + 1, 48)
                            done(dve, n_to, s, 1)
                            dve.tensor_copy(srcf[:, :], src_s[:, j, :]).then_inc(n_srcf, 1)
                            done(dve, n_hot, s, 1)
                            dve.tensor_tensor(rel[:, :, :], dst0[:, bass.ds(s * 2, 2), :],
                                              near0[:, bass.ds(s * 2, 2), None].to_broadcast([P, 2, TH]),
                                              ALU.subtract).then_inc(n_rel, 1)
                            done(dve, n_srcf, s)
                            done(dve, n_psn, s, 2)
                            for t in range(TS):
                                last = dve.tensor_scalar(same[:, k, t, :], rows[:, t // TH, t % TH, :], srcf[:, t:t + 1], None,
                                                         ALU.is_equal)
                            last.then_inc(n_same, 1)
                            done(dve, n_rel, s)
                            for t in range(TS):
                                last = dve.tensor_scalar(hot[:, k, t, :], iota_f[:, 0:W],
                                                         rel[:, t // TH, t % TH:t % TH + 1], ew_s[:, j, t:t + 1],
                                                         ALU.is_equal, ALU.mult)
                            last.then_inc(n_hot, 1)
                            done(dve, n_before, s, 1)
                            done(dve, n_away2, s, 1)
                            for t in range(TS):
                                last = dve.scalar_tensor_tensor(out=junk[:, t, :], in0=rows[:, t // TH, t % TH, :],
                                                                scalar=srcf[:, t:t + 1], in1=lower[:, :],
                                                                op0=ALU.is_equal, op1=ALU.mult,
                                                                accum_out=before[:, t:t + 1])
                            last.then_inc(n_before, 1)
                            dve.tensor_scalar(away[:, 0, :], srcf[:, :], -1.0, spare[:, 0:1], ALU.mult, ALU.add).then_inc(n_away, 1)
                            done(dve, n_before, s)
                            done(dve, n_away, s)
                            dve.scalar_tensor_tensor(out=away[:, 1, :], in0=before[:, :], scalar=1.0, in1=away[:, 0, :],
                                                     op0=ALU.min, op1=ALU.mult).then_inc(n_away2, 1)
                            done(dve, n_away2, s)
                            done(dve, n_scat, s, 3)
                            dve.tensor_tensor(to_i[:, j, :], away[:, 1, :], srcf[:, :], ALU.add).then_inc(n_to, 1)
                        sweep(dve, body, 0, NSG, 4, 192)
                        dve.tensor_scalar(base[:, :], base[:, :], float(W), None, ALU.add).then_inc(n_bases, 1)
                        dve.wait_ge(n_bases, 1)
                        dve.tensor_tensor(past[:, :, :], dst0[:, :, :], base[:, :, None].to_broadcast([P, NH, TH]),
                                          ALU.is_lt).then_inc(n_bases, 1)
                        dve.tensor_scalar(near0[:, :], base[:, :], float(N - W), None, ALU.min).then_inc(n_bases, 1)
                        dve.wait_ge(n_bases, 3)
                        dve.scalar_tensor_tensor(out=dst0[:, :, :], in0=past[:, :, :], scalar=FAR, in1=dst0[:, :, :],
                                                 op0=ALU.mult, op1=ALU.add).then_inc(n_bases, 1)
                        dve.tensor_copy(near_i[:, :], near0[0:1, :]).then_inc(n_bases, 1)
                        dve.wait_ge(n_bases, 5)

                    @block.tensor
                    def _(pe):
                        def body(s, q, j):
                            if live_sg(s):
                                k = j % 2
                                done(pe, n_same, s)
                                done(pe, n_hot, s)
                                done(pe, n_near, s, 2)
                                for t in range(TS):
                                    last = pe.matmul(ps_n[2 * k + t // TH][:, t % TH, :], hot[:, k, t, :], same[:, k, t, :],
                                                     start=True, stop=True)
                                last.then_inc(n_psn, 1)
                            m, r, i = at(s, q, j, 1)
                            if live_sg(m):
                                k = i % 2
                                done(pe, n_near, m)
                                uses(pe, xw_ld[i], r + 1, 32)
                                done(pe, n_vals, m, 2)
                                for t in range(TS):
                                    last = pe.matmul(ps_v[2 * k + t // TH][:, t % TH, :], near[:, k, t, :], xw_s[:, i, t // TH, :],
                                                     start=True, stop=True)
                                last.then_inc(n_psv, 1)
                        sweep(pe, body, 0, NSG + 1, 4, 192)

                    @block.scalar
                    def _(act):
                        def body(s, q, j):
                            if live_sg(s):
                                k = j % 2
                                done(act, n_psn, s)
                                done(act, n_psv, s, 2)
                                act.copy(near[:, k, 0:TH, :], ps_n[2 * k][:, :, :])
                                act.copy(near[:, k, TH:TS, :], ps_n[2 * k + 1][:, :, :]).then_inc(n_near, 1)
                            m, r, i = at(s, q, j, 1)
                            if live_sg(m):
                                k = i % 2
                                done(act, n_psv, m)
                                done(act, n_scat, m, 3)
                                act.copy(vals[:, i, 0:TH, :], ps_v[2 * k][:, :, :])
                                act.copy(vals[:, i, TH:TS, :], ps_v[2 * k + 1][:, :, :]).then_inc(n_vals, 1)
                        sweep(act, body, 0, NSG + 1, 4, 192)

                    @block.gpsimd
                    def _(pool):
                        def body(s, q, j):
                            done(pool, n_to, s)
                            done(pool, n_vals, s)
                            for t in range(TS):
                                i = t % NTAB
                                if not isinstance(s, int) or s * PER + t // NTAB > 0:
                                    pool.wait_ge(added[i], s * (16 * PER) + 16 * (t // NTAB))
                                settle(pool, n_scat if t == TS - 1 else passed)
                                pool.indirect_dma_start(
                                    out=sums_d[i], out_offset=bass.IndirectOffsetOnAxis(ap=to_i[:, j, t:t + 1], axis=0),
                                    in_=vals[:, j, t, :], in_offset=None, compute_op=ALU.add).then_inc(added[i], 16)
                        sweep(pool, body, 0, NSG, 4, 192)
                        for i in range(NTAB):
                            pool.wait_ge(added[i], 16 * PER * NSG)
                nums = sorted(x.num for x in sems0)
                assert nums == list(range(nums[0], nums[0] + len(nums)))
                nc.all_engine_barrier(sems_to_clear=range(nums[0], nums[0] + len(nums)))

        with ExitStack() as s3:
            def tmp(name, shape, dt=F32):
                return s3.enter_context(nc.sbuf_tensor(name, shape, dt))
            b_in = tmp("b_in", [NP, UN, CB, D])
            t_in = tmp("t_in", [NP, 2, NTAB, CB, D])
            nT = tmp("nT", [P, 2, CB, NP])
            h = tmp("h_m", [NP, 2, CB, D])
            y = tmp("y_m", [NP, 2, CB, D])
            pack = tmp("pack", [NP, UN, CB, 3, D])
            x1T = tmp("x1T", [P, 2, CB, NP])
            st6 = tmp("st6_m", [NP, 2, CB, 6])
            mv = tmp("mv_m", [NP, 2, CB, 2])
            var = tmp("var_m", [NP, 2, CB])
            sd = tmp("sd_m", [NP, 2, CB])
            r0 = tmp("r0_m", [NP, 2, CB])
            nw = tmp("nw_m", [NP, 2, 2, CB])
            rs = tmp("rs_m", [NP, 2, CB])
            ps_m = [bank(f"ps_mm{i}", [NP, CB, D], s3) for i in range(2)]
            ps_n = bank("ps_mn", [P, CB, P], s3)
            ps_t = bank("ps_mt", [P, CB, P], s3)
            ps_f = [bank(f"ps_mf{i}", [NP, CB, 2 * D], s3) for i in range(2)]
            b_ld = [sem(f"m_b_ld{i}") for i in range(UN)]
            pk_st = [sem(f"m_pk_st{i}") for i in range(UN)]
            t_ld = [sem(f"m_t_ld{i}") for i in range(UN)]
            m_sum = sem("m_sum")
            m_nT, m_mm, m_relu = sem("m_nT"), sem("m_mm"), sem("m_relu")
            m_st = [sem("m_stat_h"), sem("m_stat_y")]
            m_var = [sem("m_var_h"), sem("m_var_y")]
            m_sd = [sem("m_sd_h"), sem("m_sd_y")]
            m_nw = [sem("m_nw_h"), sem("m_nw_y")]
            m_rs = [sem("m_rs_h"), sem("m_rs_y")]
            m_cen, m_hs, m_y, m_x1 = sem("m_cen"), sem("m_hs"), sem("m_y"), sem("m_x1")
            m_tr, m_x1T, m_f, m_pk = sem("m_tr"), sem("m_x1T"), sem("m_f"), sem("m_pk")

            with nc.Block() as block:
                @block.sync
                def _(sp):
                    def body(b, q, j):
                        if live(b):
                            done(sp, m_sum, b, 2)
                            for i in range(NTAB):
                                sp.dma_start(t_in[:, j % 2, i, :, :], rows_of(sums_d[i], b)).then_inc(t_ld[j], 16)
                            done(sp, m_y, b, UN)
                            sp.dma_start(b_in[:, j, :, :], rows_of(base_d, b)).then_inc(b_ld[j], 16)
                        m, r, i = at(b, q, j, 6)
                        if live(m):
                            done(sp, m_pk, m)
                            sp.dma_start(rows_of(xs_d, m),
                                         pack[:, i, :, 0:2, :].rearrange("p c g d -> p c (g d)")).then_inc(pk_st[i], 16)
                            sp.dma_start(rows_of(f_d, m), pack[:, i, :, 2, :]).then_inc(pk_st[i], 16)
                    sweep(sp, body, 0, NB + 6, 8, 24)
                    for i in range(UN):
                        sp.wait_ge(pk_st[i], 32 * len(range(i, NB, UN)))

                @block.gpsimd
                def _(pool):
                    def body(b, q, j):
                        m, r, i = at(b, q, j, 3)
                        if live(m):
                            done(pool, m_cen, m)
                            done(pool, m_x1, m, 2)
                            pool.tensor_tensor(y[:, i % 2, :, :], h[:, i % 2, :, :],
                                               vecs[0:NP, 1, None, :].to_broadcast([NP, CB, D]), ALU.mult).then_inc(m_hs, 1)
                            done(pool, m_hs, m)
                            uses(pool, b_ld[i], r + 1, 16)
                            pool.tensor_tensor(y[:, i % 2, :, :], y[:, i % 2, :, :], b_in[:, i, :, :], ALU.add).then_inc(m_y, 1)
                    sweep(pool, body, 0, NB + 3, 4, 24)

                @block.tensor
                def _(pe):
                    def body(s, q, j):
                        b = s
                        if live(b):
                            uses(pe, t_ld[j], q + 1, 16 * NTAB)
                            done(pe, m_nT, b, 1)
                            for c in range(CB):
                                for i in range(NTAB):
                                    last = pe.matmul(ps_n[:, c, 0:NP], t_in[:, j % 2, i, c, :], ident[0:NP, 0:NP],
                                                     start=(i == 0), stop=(i == NTAB - 1))
                            last.then_inc(m_sum, 1)
                        b, r, i = at(s, q, j, 1)
                        if live(b):
                            k = i % 2
                            done(pe, m_nT, b)
                            done(pe, m_relu, b, 2)
                            pe.matmul(ps_m[k][:, :, :], ones[0:1, 0:NP], bias4[:, 1, :, :], start=True, stop=False,
                                      skip_group_check=True)
                            for c in range(CB):
                                last = pe.matmul(ps_m[k][:, c, :], nT[:, k, c, :], neigh_wT[:, :],
                                                 start=False, stop=(c == CB - 1), skip_group_check=True)
                            last.then_inc(m_mm, 1)
                        m, r, i = at(s, q, j, 4)
                        if live(m):
                            done(pe, m_x1, m)
                            done(pe, m_x1T, m, 1)
                            for c in range(CB):
                                last = pe.transpose(ps_t[:, c, 0:NP], pack[:, i, c, 0, :], ident[0:NP, 0:NP])
                            last.then_inc(m_tr, 1)
                        m, r, i = at(s, q, j, 5)
                        if live(m):
                            done(pe, m_x1T, m)
                            done(pe, m_pk, m, 2)
                            for c in range(CB):
                                last = pe.matmul(ps_f[i % 2][:, c, :], x1T[:, i % 2, c, :], node_w[:, :], start=True, stop=True)
                            last.then_inc(m_f, 1)
                    sweep(pe, body, 0, NB + 5, 8, 24)

                @block.scalar
                def _(act):
                    def root(m, which):
                        if live(m):
                            done(act, m_var[which], m)
                            done(act, m_rs[which], m, 1)
                            act.activation(sd[:, which, :], var[:, which, :], ACT.Sqrt).then_inc(m_sd[which], 1)

                    def body(b, q, j):
                        if live(b):
                            done(act, m_sum, b)
                            done(act, m_mm, b, 2)
                            act.copy(nT[:, j % 2, :, :], ps_n[:, :, 0:NP]).then_inc(m_nT, 1)
                        m, r, i = at(b, q, j, 1)
                        if live(m):
                            done(act, m_mm, m)
                            done(act, m_hs, m, 2)
                            act.activation(h[:, i % 2, :, :], ps_m[i % 2][:, :, :], ACT.Relu).then_inc(m_relu, 1)
                        root(b - 2, 0)
                        root(b - 3, 1)
                        m, r, i = at(b, q, j, 4)
                        if live(m):
                            done(act, m_tr, m)
                            done(act, m_f, m, 2)
                            act.copy(x1T[:, i % 2, :, :], ps_t[:, :, 0:NP]).then_inc(m_x1T, 1)
                    sweep(act, body, 0, NB + 4, 8, 24)

                @block.vector
                def _(dve):
                    def statistics(m, rows, which, eps):
                        for c in range(CB):
                            last = dve.bn_stats(st6[:, which, c, :], rows[:, c, :])
                        last.then_inc(m_st[which], 1)
                        dve.wait_ge(m_st[which], m * 2 + 1)
                        settle(dve, passed)
                        for c in range(CB):
                            last = dve.bn_aggr(mv[:, which, c, :], st6[:, which, c, :])
                        last.then_inc(m_st[which], 1)
                        dve.wait_ge(m_st[which], m * 2 + 2)
                        done(dve, m_sd[which], m, 1)
                        dve.tensor_scalar(var[:, which, :], mv[:, which, :, 1], eps, None, ALU.add).then_inc(m_var[which], 1)

                    def centre(m, rows, to, which):
                        done(dve, m_sd[which], m)
                        dve.reciprocal(r0[:, which, :], sd[:, which, :]).then_inc(m_rs[which], 1)
                        done(dve, m_rs[which], m)
                        refine(dve, var[:, which, :], r0[:, which, :], nw[:, which, :, :], rs[:, which, :], m_nw[which], m)
                        for c in range(CB):
                            last = dve.tensor_scalar(to[:, c, :], rows[:, c, :], mv[:, which, c, 0:1], rs[:, which, c:c + 1],
                                                     ALU.subtract, ALU.mult)
                        return last

                    def body(b, q, j):
                        m1, r1, i1 = at(b, q, j, 2)
                        m2, r2, i2 = at(b, q, j, 3)
                        m4, r4, i4 = at(b, q, j, 5)
                        if live(m1):
                            done(dve, m_relu, m1)
                            statistics(m1, h[:, i1 % 2, :, :], 0, 1e-9)
                        if live(m2):
                            done(dve, m_y, m2)
                            statistics(m2, y[:, i2 % 2, :, :], 1, 1e-5)
                        if live(m4):
                            done(dve, m_f, m4)
                            for g in range(2):
                                last = dve.tensor_tensor(
                                    pack[:, i4, :, 1 + g, :], ps_f[i4 % 2][:, :, g * D:(g + 1) * D],
                                    attr_s[:, bass.ds(m4 * CB, CB), None].to_broadcast([NP, CB, D]), ALU.mult)
                            last.then_inc(m_pk, 1)
                        if live(m1):
                            k = i1 % 2
                            centre(m1, h[:, k, :, :], h[:, k, :, :], 0).then_inc(m_cen, 1)
                        if live(m2):
                            uses(dve, pk_st[i2], r2, 32)
                            centre(m2, y[:, i2 % 2, :, :], pack[:, i2, :, 0, :], 1).then_inc(m_x1, 1)
                    sweep(dve, body, 0, NB + 5, 8, 24)

        with ExitStack() as s4:
            def tmp(name, shape, dt=F32):
                return s4.enter_context(nc.sbuf_tensor(name, shape, dt))
            src_s = tmp("src_e", [P, UN, TS], I32)
            e4_s = tmp("e4_s", [P, UN, TS, 4])
            e64_s = tmp("e64_s", [P, UN, TS, EF])
            fg = tmp("fg", [P, UN, TS, D])
            rel = tmp("rel1", [P, 2, TH])
            raw = tmp("raw", [P, TS, W])
            hot = tmp("hot1", [P, 2, TS, 4, W])
            prod = tmp("prod", [P, 2, TS, 2, D])
            eT = tmp("eT", [P, 2, TS // 2, P])
            sig = tmp("sig", [P, 2, TS // 2, P])
            hid = tmp("hid", [P, 2, TS // 2, P])
            sums = tmp("sums", [P, 2, 2, 4, W])
            sums_a = tmp("sums_a", [P, 2, 2, W])
            ps_t = bank("ps_et", [P, TS // 2, P], s4)
            ps_h = bank("ps_eh", [P, TS // 2, P], s4)
            ps_w = [bank(f"ps_ew{i}", [P, TS, 4, MUL], s4) for i in range(2)]
            ps_u = bank("ps_eu", [P, 2, 4, W], s4)
            ps_c = bank("ps_ec", [P, 2, 2, W], s4)
            src_ld = [sem(f"e_src_ld{i}") for i in range(UN)]
            e4_ld = [sem(f"e_e4_ld{i}") for i in range(UN)]
            e64_ld = [sem(f"e_e64_ld{i}") for i in range(UN)]
            gath = [sem(f"e_gath{i}") for i in range(UN)]
            e_tr, e_eT, e_fc1, e_sig, e_hid, e_fc2 = (sem("e_tr"), sem("e_eT"), sem("e_fc1"), sem("e_sig"), sem("e_hid"),
                                                      sem("e_fc2"))
            e_rel, e_raw, e_hot, e_prod = sem("e_rel"), sem("e_raw"), sem("e_hot"), sem("e_prod")
            e_seg, e_sums, e_lin, e_add1, e_add = sem("e_seg"), sem("e_sums"), sem("e_lin"), sem("e_add1"), sem("e_add")
            e_bases, clear_d = sem("e_bases"), sem("e_clear")
            sems1 = src_ld + e4_ld + e64_ld + gath + [e_tr, e_eT, e_fc1, e_sig, e_hid, e_fc2, e_rel, e_raw, e_hot, e_prod,
                                                      e_seg, e_sums, e_lin, e_add1, e_add, e_bases]
            with nc.Block() as block:
                @block.vector
                def _(dve):
                    dve.tensor_copy(base[:, :], base0[:, :])
                    dve.tensor_copy(base_i[:, :], base0[0:1, :]).then_inc(clear_d, 1)
                    dve.wait_ge(clear_d, 1)

            npass = nc.values_load(npass_i[0:1, 0:1], min_val=1, max_val=N // W + 1)
            with nc.Fori(0, npass):
                with nc.Block() as block:
                    @block.sync
                    def _(sp):
                        def body(s, q, j):
                            e0 = first_edge(sp, s)
                            uses(sp, gath[j], q, 16 * TS)
                            settle(sp, passed)
                            done(sp, e_hot, s, UN)
                            done(sp, e_tr, s, UN)
                            sp.dma_start(src_s[:, j, :].rearrange("p (h k) -> p h k", h=2),
                                         edges_of(a["src"], e0, False)).then_inc(src_ld[j], 16)
                            sp.dma_start(e64_s[:, j, :, :].rearrange("p (h k) e -> p h (k e)", h=2),
                                         edges_of(a["edge_attr_64"], e0, True)).then_inc(e64_ld[j], 16)
                            sp.dma_start(e4_s[:, j, :, :].rearrange("p (h k) e -> p h (k e)", h=2),
                                         edges_of(a["edge_attr_4"], e0, True)).then_inc(e4_ld[j], 16)
                        sweep(sp, body, 0, NSG, 4, 192)

                    @block.gpsimd
                    def _(pool):
                        def body(s, q, j):
                            uses(pool, src_ld[j], q + 1, 16)
                            done(pool, e_prod, s, UN)
                            settle(pool, passed)
                            for t in range(TS):
                                pool.indirect_dma_start(
                                    out=fg[:, j, t, :], out_offset=None, in_=f_d,
                                    in_offset=bass.IndirectOffsetOnAxis(ap=src_s[:, j, t:t + 1], axis=0)).then_inc(gath[j], 16)
                        sweep(pool, body, 0, NSG, 4, 192)

                    @block.tensor
                    def _(pe):
                        def body(s, q, j):
                            if live_sg(s):
                                k = j % 2
                                done(pe, e_hid, s)
                                done(pe, e_prod, s, 2)
                                for t in range(TS // 2):
                                    last = pe.matmul(ps_w[k][:, 2 * t:2 * t + 2, :, :], hid[:, k, t, :], fc2_w[:, :],
                                                     start=True, stop=True)
                                last.then_inc(e_fc2, 1)
                            m, r, i = at(s, q, j, -2)
                            if live_sg(m):
                                uses(pe, e64_ld[i], r + 1, 16)
                                done(pe, e_eT, m, 1)
                                for t in range(TS // 2):
                                    last = pe.transpose(ps_t[:, t, :], e64_s[:, i, 2 * t:2 * t + 2, :].rearrange("p t e -> p (t e)"),
                                                        ident[:, :])
                                last.then_inc(e_tr, 1)
                            m, r, i = at(s, q, j, -1)
                            if live_sg(m):
                                done(pe, e_eT, m)
                                done(pe, e_hid, m, 1)
                                pe.matmul(ps_h[:, :, :], fc1_w[:, :], eT[:, i % 2, :, :], start=True, stop=True).then_inc(e_fc1, 1)
                            m, r, i = at(s, q, j, 1)
                            if live_sg(m):
                                k = i % 2
                                done(pe, e_prod, m)
                                done(pe, e_hot, m)
                                done(pe, e_sums, m, 1)
                                for t in range(TS):
                                    hf = t // TH
                                    pe.matmul(ps_u[:, hf, 0, :], prod[:, k, t, 0, :], hot[:, k, t, 0, :],
                                              start=(t == 0), stop=False, skip_group_check=True)
                                    last = pe.matmul(ps_u[:, hf, 1:4, :], prod[:, k, t, 1, :], hot[:, k, t, 1:4, :],
                                                     start=False, stop=(t == TS - 1), skip_group_check=True)
                                last.then_inc(e_seg, 1)
                            m, r, i = at(s, q, j, 2)
                            if live_sg(m):
                                k = i % 2
                                done(pe, e_sums, m)
                                done(pe, e_add, m, 1)
                                for c in range(4):
                                    pe.matmul(ps_c[:, 0, :, :], lin_w[:, c, :], sums[:, k, :, c, :], start=(c == 0), stop=(c == 3))
                                last = pe.matmul(ps_c[:, 1, :, :], lin_w[:, 4, :], sums_a[:, k, :, :], start=True, stop=True)
                                last.then_inc(e_lin, 1)
                        sweep(pe, body, -2, NSG + 2, 4, 192)

                    @block.scalar
                    def _(act):
                        def body(s, q, j):
                            m, r, i = at(s, q, j, -2)
                            if live_sg(m):
                                done(act, e_tr, m)
                                done(act, e_fc1, m, 2)
                                act.copy(eT[:, i % 2, :, :], ps_t[:, :, :]).then_inc(e_eT, 1)
                            m, r, i = at(s, q, j, -1)
                            if live_sg(m):
                                done(act, e_fc1, m)
                                done(act, e_hid, m, 2)
                                act.activation(sig[:, i % 2, :, :], ps_h[:, :, :], ACT.Sigmoid).then_inc(e_sig, 1)
                            m, r, i = at(s, q, j, 1)
                            if live_sg(m):
                                done(act, e_seg, m)
                                done(act, e_lin, m, 2)
                                for c in range(4):
                                    act.copy(sums_a[MUL * c:MUL * (c + 1), i % 2, :, :], ps_u[MUL * c:MUL * (c + 1), :, c, :])
                                act.copy(sums[:, i % 2, :, :, :], ps_u[:, :, :, :]).then_inc(e_sums, 1)
                        sweep(act, body, -2, NSG + 1, 4, 192)

                    @block.vector
                    def _(dve):
                        def body(s, q, j):
                            if live_sg(s):
                                k = j % 2
                                uses(dve, e4_ld[j], q + 1, 16)
                                done(dve, e_raw, s, 1)
                                dve.tensor_tensor(rel[:, :, :], dstf[:, bass.ds(s * 2, 2), :],
                                                  base[:, bass.ds(s * 2, 2), None].to_broadcast([P, 2, TH]),
                                                  ALU.subtract).then_inc(e_rel, 1)
                                done(dve, e_rel, s)
                                done(dve, e_hot, s, 1)
                                dve.tensor_tensor(raw[:, :, :], iota_f[:, None, 0:W].to_broadcast([P, TS, W]),
                                                  rel[:, :, :].rearrange("p h k -> p (h k)")[:, :, None].to_broadcast([P, TS, W]),
                                                  ALU.is_equal).then_inc(e_raw, 1)
                                done(dve, e_raw, s)
                                done(dve, e_seg, s, 2)
                                dve.tensor_tensor(hot[:, k, :, :, :], raw[:, :, None, :].to_broadcast([P, TS, 4, W]),
                                                  e4_s[:, j, :, :, None].to_broadcast([P, TS, 4, W]),
                                                  ALU.mult).then_inc(e_hot, 1)
                                done(dve, e_fc2, s)
                                uses(dve, gath[j], q + 1, 16 * TS)
                                for g in range(2):
                                    dve.tensor_tensor(prod[:, k, :, g, 0:MUL], ps_w[k][:, :, g, :], fg[:, j, :, 0:MUL], ALU.mult)
                                    last = dve.tensor_tensor(
                                        prod[:, k, :, g, MUL:D].rearrange("p t (d u) -> p t d u", d=3),
                                        ps_w[k][:, :, 2 + g, None, :].to_broadcast([P, TS, 3, MUL]),
                                        fg[:, j, :, MUL:D].rearrange("p t (d u) -> p t d u", d=3), ALU.mult)
                                last.then_inc(e_prod, 1)
                            m, r, i = at(s, q, j, -1)
                            if live_sg(m):
                                done(dve, e_sig, m)
                                done(dve, e_fc2, m, 2)
                                dve.scalar_tensor_tensor(out=hid[:, i % 2, :, :], in0=sig[:, i % 2, :, :], scalar=1.679,
                                                         in1=ps_h[:, :, :], op0=ALU.mult, op1=ALU.mult).then_inc(e_hid, 1)
                            m, r, i = at(s, q, j, 3)
                            if live_sg(m):
                                b0 = dve.value_load(base_i[0:1, bass.ds(m * 2, 1)], min_val=0, max_val=N)
                                b1 = dve.value_load(base_i[0:1, bass.ds(m * 2 + 1, 1)], min_val=0, max_val=N)
                                done(dve, e_lin, m)
                                done(dve, e_add, m, 1)
                                to = table[:, :, bass.ds(b0, W)]
                                dve.tensor_tensor(to, ps_c[:, :, 0, :], to, ALU.add).then_inc(e_add1, 1)
                                done(dve, e_add1, m)
                                to = table[:, :, bass.ds(b1, W)]
                                dve.tensor_tensor(to, ps_c[:, :, 1, :], to, ALU.add).then_inc(e_add, 1)
                        sweep(dve, body, -1, NSG + 3, 4, 192)
                        dve.tensor_scalar(base[:, :], base[:, :], float(W), None, ALU.add).then_inc(e_bases, 1)
                        dve.wait_ge(e_bases, 1)
                        dve.tensor_scalar(base_i[:, :], base[0:1, :], float(N), None, ALU.min).then_inc(e_bases, 1)
                        dve.wait_ge(e_bases, 2)
                nums = sorted(x.num for x in sems1)
                assert nums == list(range(nums[0], nums[0] + len(nums)))
                nc.all_engine_barrier(sems_to_clear=range(nums[0], nums[0] + len(nums)))

        with ExitStack() as s5:
            def tmp(name, shape, dt=F32):
                return s5.enter_context(nc.sbuf_tensor(name, shape, dt))
            sin_a = tmp("sin_a", [NP, NB * CB])
            cos_a = tmp("cos_a", [NP, NB * CB])
            ang_r = tmp("ang_r", [NB * CB, NP])
            th = tmp("th", [NP, NB * CB])
            k2 = tmp("k2", [NP, NB * CB])
            r1 = tmp("r1", [NP, 2, NB * CB])
            over = tmp("over", [NP, NB * CB])
            trig = tmp("trig", [NP, 2, NB * CB])
            c_in = tmp("c_in", [P, 2, BN])
            xs_in = tmp("xs_in", [NP, UN, CB, 2, D])
            t_sb = tmp("t_sb", [NP, 2, CB, D])
            y = tmp("y_f", [NP, 2, CB, D])
            o_sb = tmp("o_sb", [NP, UN, CB, D])
            st6 = tmp("st6_f", [NP, CB, 6])
            mv = tmp("mv_f", [NP, 2, CB, 2])
            var = tmp("var_f", [NP, CB])
            sd = tmp("sd_f", [NP, CB])
            r0 = tmp("r0_f", [NP, CB])
            nw = tmp("nw_f", [NP, 2, CB])
            rs = tmp("rs_f", [NP, CB])
            ps_a = bank("ps_fa", [NP, NB * CB], s5)
            ps_c = [bank(f"ps_fc{i}", [NP, CB, D], s5) for i in range(2)]
            a_out, a_in, a_T, a_step, a_arg, a_trig = (sem("a_out"), sem("a_in"), sem("a_T"), sem("a_step"), sem("a_arg"),
                                                       sem("a_trig"))
            with nc.Block() as block:
                @block.sync
                def _(sp):
                    sp.dma_start(ang_d, table[0:1, 1, 0:N]).then_inc(a_out, 16)
                    sp.wait_ge(a_out, 16)
                    sp.dma_start(ang_r[:, :], ang_d.rearrange("o (t p) -> (o t) p", p=NP)).then_inc(a_in, 16)

                @block.tensor
                def _(pe):
                    pe.wait_ge(a_in, 16)
                    pe.transpose(ps_a[:, :], ang_r[:, :], ident[0:NB * CB, 0:NB * CB]).then_inc(a_T, 1)

                @block.vector
                def _(dve):
                    step = 0

                    def link(ins):
                        nonlocal step
                        step += 1
                        ins.then_inc(a_step, 1)
                        dve.wait_ge(a_step, step)
                    dve.wait_ge(a_T, 1)
                    link(dve.tensor_scalar(th[:, :], ps_a[:, :], 0.1, None, ALU.mult))
                    link(dve.scalar_tensor_tensor(out=th[:, :], in0=th[:, :], scalar=1.0 / 32.0, in1=attr[:, :],
                                                  op0=ALU.mult, op1=ALU.mult))
                    link(dve.tensor_scalar(k2[:, :], th[:, :], 0.15915494309189535, ROUND, ALU.mult, ALU.add))
                    link(dve.tensor_scalar(k2[:, :], k2[:, :], ROUND, None, ALU.subtract))
                    for part in TWO_PI:
                        link(dve.scalar_tensor_tensor(out=th[:, :], in0=k2[:, :], scalar=-part, in1=th[:, :],
                                                      op0=ALU.mult, op1=ALU.add))
                    link(dve.tensor_scalar(r1[:, 0, :], th[:, :], PI, -PI, ALU.min, ALU.max))
                    link(dve.tensor_scalar(th[:, :], th[:, :], 1.5707963267948966, None, ALU.add))
                    link(dve.tensor_scalar(over[:, :], th[:, :], PI, -6.283185307179586, ALU.is_gt, ALU.mult))
                    link(dve.tensor_tensor(th[:, :], th[:, :], over[:, :], ALU.add))
                    dve.tensor_scalar(r1[:, 1, :], th[:, :], PI, -PI, ALU.min, ALU.max).then_inc(a_arg, 1)
                    dve.wait_ge(a_trig, 1)
                    dve.tensor_copy(cos_a[:, :], trig[:, 1, :])
                    link(dve.tensor_tensor(sin_a[:, :], trig[:, 0, :], attr[:, :], ALU.mult))
                    link(dve.tensor_scalar(sin_a[:, :], sin_a[:, :], 1.0 / 32.0, None, ALU.mult))

                @block.scalar
                def _(act):
                    act.wait_ge(a_arg, 1)
                    act.activation(trig[:, :, :], r1[:, :, :], ACT.Sin).then_inc(a_trig, 1)

            xs_ld = [sem(f"f_xs_ld{i}") for i in range(UN)]
            o_st = [sem(f"f_o_st{i}") for i in range(UN)]
            f_c, f_tr, f_t0, f_t, f_u, f_y = sem("f_c"), sem("f_tr"), sem("f_t0"), sem("f_t"), sem("f_u"), sem("f_y")
            f_st, f_var, f_sd, f_rs, f_nw, f_o = sem("f_st"), sem("f_var"), sem("f_sd"), sem("f_rs"), sem("f_nw"), sem("f_o")
            with nc.Block() as block:
                @block.sync
                def _(sp):
                    def body(b, q, j):
                        if live(b):
                            done(sp, f_t, b, UN)
                            sp.dma_start(xs_in[:, j, :, :, :].rearrange("p c g d -> p c (g d)"), rows_of(xs_d, b)).then_inc(xs_ld[j], 16)
                        m, r, i = at(b, q, j, 2)
                        if live(m):
                            done(sp, f_o, m)
                            sp.dma_start(rows_of(out, m), o_sb[:, i, :, :]).then_inc(o_st[i], 16)
                    sweep(sp, body, 0, NB + 2, 4, 24)
                    for i in range(UN):
                        sp.wait_ge(o_st[i], 16 * len(range(i, NB, UN)))

                @block.gpsimd
                def _(pool):
                    def body(b, q, j):
                        k = j % 2
                        done(pool, f_tr, b, 2)
                        pool.tensor_copy(c_in[:, k, :], table[:, 0, bass.ds(b * BN, BN)]).then_inc(f_c, 1)
                        uses(pool, xs_ld[j], q + 1, 16)
                        done(pool, f_y, b, 2)
                        pool.tensor_tensor(t_sb[:, k, :, :], xs_in[:, j, :, 1, :],
                                           cos_a[:, bass.ds(b * CB, CB), None].to_broadcast([NP, CB, D]), ALU.mult).then_inc(f_t0, 1)
                        done(pool, f_t0, b)
                        pool.tensor_tensor(t_sb[:, k, :, :], t_sb[:, k, :, :], xs_in[:, j, :, 0, :], ALU.add).then_inc(f_t, 1)
                    sweep(pool, body, 0, NB, 4, 24)

                @block.tensor
                def _(pe):
                    def body(b, q, j):
                        done(pe, f_c, b)
                        done(pe, f_u, b, 2)
                        for c in range(CB):
                            last = pe.transpose(ps_c[j % 2][:, c, :], c_in[:, j % 2, NP * c:NP * (c + 1)], ident[:, :])
                        last.then_inc(f_tr, 1)
                    sweep(pe, body, 0, NB, 4, 24)

                @block.scalar
                def _(act):
                    def body(b, q, j):
                        done(act, f_var, b)
                        done(act, f_rs, b, 1)
                        act.activation(sd[:, :], var[:, :], ACT.Sqrt).then_inc(f_sd, 1)
                    sweep(act, body, 0, NB, 4, 24)

                @block.vector
                def _(dve):
                    def body(b, q, j):
                        if live(b):
                            k = j % 2
                            done(dve, f_tr, b)
                            done(dve, f_o, b, 2)
                            dve.tensor_tensor(y[:, k, :, :], ps_c[k][:, :, :],
                                              sin_a[:, bass.ds(b * CB, CB), None].to_broadcast([NP, CB, D]), ALU.mult).then_inc(f_u, 1)
                            done(dve, f_u, b)
                            done(dve, f_t, b)
                            dve.tensor_tensor(y[:, k, :, :], y[:, k, :, :], t_sb[:, k, :, :], ALU.add).then_inc(f_y, 1)
                            done(dve, f_y, b)
                            for c in range(CB):
                                last = dve.bn_stats(st6[:, c, :], y[:, k, c, :])
                            last.then_inc(f_st, 1)
                        m, r, i = at(b, q, j, 1)
                        if live(m):
                            done(dve, f_sd, m)
                            dve.reciprocal(r0[:, :], sd[:, :]).then_inc(f_rs, 1)
                            done(dve, f_rs, m)
                            refine(dve, var[:, :], r0[:, :], nw, rs[:, :], f_nw, m)
                            uses(dve, o_st[i], r, 16)
                            for c in range(CB):
                                last = dve.tensor_scalar(o_sb[:, i, c, :], y[:, i % 2, c, :], mv[:, i % 2, c, 0:1],
                                                         rs[:, c:c + 1], ALU.subtract, ALU.mult)
                            last.then_inc(f_o, 1)
                        if live(b):
                            dve.wait_ge(f_st, b * 2 + 1)
                            settle(dve, passed)
                            for c in range(CB):
                                last = dve.bn_aggr(mv[:, j % 2, c, :], st6[:, c, :])
                            last.then_inc(f_st, 1)
                            dve.wait_ge(f_st, b * 2 + 2)
                            done(dve, f_sd, b, 1)
                            dve.tensor_scalar(var[:, :], mv[:, j % 2, :, 1], 1e-5, None, ALU.add).then_inc(f_var, 1)
                    sweep(dve, body, 0, NB + 1, 4, 24)


_INS = ["x", "src", "dst", "edge_attr_4", "edge_attr_64", "edge_weight", "node_vec1", "L0_gnn_W_self", "L0_gnn_b_self",
        "L0_gnn_W_neigh", "L0_gnn_b_neigh", "L0_gnn_scale", "L0_gnn_offset", "L1_gnn_W_sc0", "L1_gnn_W_sc1",
        "L1_gnn_W_l1_0", "L1_gnn_W_l1_1", "L1_gnn_W_fc1", "L1_gnn_W_fc2", "L1_gnn_W_l2_A0", "L1_gnn_W_l2_B0",
        "L1_gnn_W_l2_C1", "L1_gnn_W_l2_D1", "L1_gnn_W_l3_A", "L1_gnn_W_l3_B"]


def kernel(**inputs):
    import numpy as np
    import concourse.bacc as bacc
    from concourse.bass_utils import run_bass_kernel_spmd

    nc = bacc.Bacc("TRN2", target_bir_lowering=False, num_devices=1)
    arrays, args = {}, {}
    for name in _INS:
        v = np.ascontiguousarray(inputs[name])
        arrays[f"in_{name}"] = v
        args[name] = nc.dram_tensor(f"in_{name}", v.shape, mybir.dt.from_np(v.dtype), kind="ExternalInput").ap()
    out = nc.dram_tensor("out", (N, D), F32, kind="ExternalOutput").ap()
    graph_layers(nc, args, out)
    return run_bass_kernel_spmd(nc, [arrays], core_ids=[0]).results[0]["out"]
```
